# Optimizing a Trainium2 kernel written in Bass

```python
import numpy as np
import jax
import jax.numpy as jnp

def _softmax(x, axis=-1):
    return jax.nn.softmax(x, axis=axis)

def _gelu(x):
    return jax.nn.gelu(x, approximate=True)

def _silu(x):
    return jax.nn.silu(x)

def _sigmoid(x):
    return jax.nn.sigmoid(x)

def _layernorm(x, axis=-1, eps=1e-05):
    m = jnp.mean(x, axis=axis, keepdims=True)
    v = jnp.var(x, axis=axis, keepdims=True)
    return (x - m) / jnp.sqrt(v + eps)

def _scatter_add(tgt, idx, src, axis=0):
    return tgt.at[idx].add(src)

def _segment_sum(src, seg, n):
    return jax.ops.segment_sum(src, seg, n)
kernel_name = 'mk_flamingo_gated_d1_seqx_r8_b95adf'

def setup_inputs(seed: int=0):
    np.random.seed(seed)
    _w = jnp.asarray

    def _rec_inputs():
        import jax
        import jax.numpy as jnp
        _rk = jax.random.key(seed)
        x = 0.0003765 + 1 * jax.random.normal(jax.random.fold_in(_rk, 1), (8, 128, 256), jnp.float32)
        _lenS = 128 - jax.random.randint(jax.random.fold_in(_rk, 7), (8,), 0, max(1, 128 // 4) + 1, jnp.int32)
        _lenS2 = 128 - jax.random.randint(jax.random.fold_in(_rk, 8), (8,), 0, max(1, 128 // 4) + 1, jnp.int32)
        _ctx_2048P = jax.random.normal(jax.random.fold_in(_rk, 11), (8, 16, 256), jnp.float32)
        _ctx_2048c = jax.random.dirichlet(jax.random.fold_in(_rk, 511), 0.3 * jnp.ones((16,), jnp.float32), (8, 128))
        _ctx_2048t = jnp.einsum('bsk,bkd->bsd', _ctx_2048c, _ctx_2048P)
        _ctx_2048t = _ctx_2048t * jax.lax.rsqrt(jnp.mean(jnp.square(_ctx_2048t)) + 1e-12) * 0.953939
        ctx_2048 = -0.000292821 + 1.00034 * (_ctx_2048t + 0.3 * jax.random.normal(jax.random.fold_in(_rk, 611), (8, 128, 256), jnp.float32))
        _g = jax.random.normal(jax.random.fold_in(_rk, 9001), (2, 1), jnp.float32)
        _g = jnp.sign(_g) * jnp.maximum(jnp.abs(_g), 1.0) + (_g == 0) * 1.0
        g_xattn = _g[0]
        g_ffn = _g[1]
        return (x, ctx_2048, g_xattn, g_ffn)
    x, ctx_2048, g_xattn, g_ffn = _rec_inputs()

    def _L0_xattn_setup():
        import jax, jax.numpy as jnp
        import numpy as np
        key = jax.random.key(seed)
        k1, k2, k3, k4, k5 = jax.random.split(key, 5)
        B, D_MODEL, L = (2, 128, 256)
        HEAD_DIM = 8
        H = D_MODEL // HEAD_DIM
        return {'k': jax.random.normal(k1, (B, D_MODEL, L), dtype=jnp.float32), 'v': jax.random.normal(k2, (B, D_MODEL, L), dtype=jnp.float32), 'q': jax.random.normal(k3, (B, D_MODEL, L), dtype=jnp.float32), 'ssm_kernel': jax.random.normal(k4, (H, L), dtype=jnp.float32), 'D': jax.random.normal(k5, (H,), dtype=jnp.float32), 'head_dim': HEAD_DIM}
    _L0_xattn_all = _L0_xattn_setup()
    _L0_xattn_in = {k: v for k, v in _L0_xattn_all.items() if k in ('ssm_kernel', 'D')}
    del _L0_xattn_all

    def _L0_ffn_setup():
        import jax, jax.numpy as jnp
        import numpy as np
        GROUP_SIZE = 64

        def ternary_quant(w_fp32, g=GROUP_SIZE):
            w = w_fp32.astype(jnp.bfloat16)
            w_g = w.reshape(-1, g)
            scale = jnp.clip(jnp.mean(jnp.abs(w_g), axis=-1, keepdims=True), 1e-08, None)
            q = jnp.clip(jnp.round(w_g / scale), -1, 1)
            w_hat = (q * scale).reshape(w.shape)
            return w + jax.lax.stop_gradient(w_hat - w)

        def rms_norm(x):
            eps = jnp.finfo(x.dtype).eps.astype(jnp.float32)
            xf = x.astype(jnp.float32)
            inv = jax.lax.rsqrt(jnp.mean(xf * xf, axis=-1, keepdims=True) + eps)
            return (xf * inv).astype(x.dtype)
        key = jax.random.key(seed)
        k1, k2, k3 = jax.random.split(key, 3)
        B, S, D = (2, 256, 256)
        H = 4 * D
        x = jax.random.normal(k1, (B, S, D), dtype=jnp.float32).astype(jnp.bfloat16)
        w_gate_up = jax.random.normal(k2, (2 * H, D), dtype=jnp.float32) * 0.02
        w_proj = jax.random.normal(k3, (D, H), dtype=jnp.float32) * 0.02
        return {'x': x, 'w_gate_up': w_gate_up, 'w_proj': w_proj}
    _L0_ffn_all = _L0_ffn_setup()
    _L0_ffn_in = {k: v for k, v in _L0_ffn_all.items() if k in ('w_gate_up', 'w_proj')}
    del _L0_ffn_all
    return {'x': x, 'ctx_2048': ctx_2048, 'g_xattn': g_xattn, 'g_ffn': g_ffn, 'L0_xattn_ssm_kernel': _L0_xattn_in['ssm_kernel'], 'L0_xattn_D': _L0_xattn_in['D'], 'L0_ffn_w_gate_up': _L0_ffn_in['w_gate_up'], 'L0_ffn_w_proj': _L0_ffn_in['w_proj']}

def reference(x, ctx_2048, g_xattn, g_ffn, L0_xattn_ssm_kernel, L0_xattn_D, L0_ffn_w_gate_up, L0_ffn_w_proj):
    import jax
    import jax.numpy as jnp

    def _L0_xattn_ref(k, v, q, ssm_kernel, D, head_dim):
        import jax, jax.numpy as jnp
        import numpy as np
        B, HD, L = k.shape
        H = HD // head_dim
        fft_size = 2 * L
        k_ = k.reshape(B, H, head_dim, L)
        v_ = v.reshape(B, H, head_dim, L)
        q_ = q.reshape(B, H, head_dim, L)
        kv = jnp.einsum('bhil,bhjl->bijhl', k_, v_)
        kv_f = jnp.fft.rfft(kv, n=fft_size)
        kernel_f = jnp.fft.rfft(ssm_kernel, n=fft_size)
        y = jnp.fft.irfft(kv_f * kernel_f, n=fft_size)[..., :L]
        out = y + kv * D[None, None, None, :, None]
        out = jnp.einsum('bijhl,bhil->bjhl', out, q_)
        out = jnp.transpose(out, (0, 2, 1, 3)).reshape(B, H * head_dim, L)
        return out.astype(k.dtype)

    def _L0_ffn_ref(x, w_gate_up, w_proj):
        import jax, jax.numpy as jnp
        import numpy as np
        GROUP_SIZE = 64

        def ternary_quant(w_fp32, g=GROUP_SIZE):
            w = w_fp32.astype(jnp.bfloat16)
            w_g = w.reshape(-1, g)
            scale = jnp.clip(jnp.mean(jnp.abs(w_g), axis=-1, keepdims=True), 1e-08, None)
            q = jnp.clip(jnp.round(w_g / scale), -1, 1)
            w_hat = (q * scale).reshape(w.shape)
            return w + jax.lax.stop_gradient(w_hat - w)

        def rms_norm(x):
            eps = jnp.finfo(x.dtype).eps.astype(jnp.float32)
            xf = x.astype(jnp.float32)
            inv = jax.lax.rsqrt(jnp.mean(xf * xf, axis=-1, keepdims=True) + eps)
            return (xf * inv).astype(x.dtype)
        wq_gu = ternary_quant(w_gate_up)
        gu = jnp.einsum('bsd,hd->bsh', x, wq_gu)
        gate, up = jnp.split(gu, 2, axis=-1)
        h = jax.nn.silu(gate) * up
        hn = rms_norm(h)
        wq_p = ternary_quant(w_proj)
        return jnp.einsum('bsh,dh->bsd', hn, wq_p)
    x = x + jnp.tanh(g_xattn[0]) * _L0_xattn_ref(ctx_2048, ctx_2048, _layernorm(x, axis=-1), L0_xattn_ssm_kernel, L0_xattn_D, 8)
    x = x + jnp.tanh(g_ffn[0]) * _L0_ffn_ref(_layernorm(x, axis=-1), L0_ffn_w_gate_up, L0_ffn_w_proj)
    return x

_drawn_inputs = setup_inputs


def setup_inputs(seed=0):
    import zlib

    import numpy as np

    out = dict(_drawn_inputs(seed))
    spreads = {}
    factors = {'L0_ffn_w_gate_up': 3.948, 'L0_ffn_w_proj': 3.956}
    for name, (base, spread) in spreads.items():
        noise = np.random.default_rng([zlib.crc32(name.encode()), seed]).standard_normal(out[name].shape)
        drawn = base * np.exp(spread * noise) if base else spread * noise
        out[name] = jnp.asarray(drawn.astype(out[name].dtype))
    for name, factor in factors.items():
        out[name] = (out[name] * factor).astype(out[name].dtype)
    return out
```

```python
from contextlib import ExitStack

import concourse.bass as bass
from concourse import mybir

ALU = mybir.AluOpType
ACT = mybir.ActivationFunctionType
AX = mybir.AxisListType
F32 = mybir.dt.float32
F16 = mybir.dt.float16
BF16 = mybir.dt.bfloat16
RMAX = bass.bass_isa.ReduceOp.max

P = 128
B, D_MODEL, L = 8, 128, 256
H, HD = 16, 8
HID = 1024
LN_EPS = 1e-5
RMS_EPS = 2.0 ** -23
NB = 4
LB = L // P
UNITS = H * LB * NB
HU = LB * NB
WRAP = 12
PAIRS = 36
ROWS_A, ROWS_B = 5, 3
WIDE = 16
HG = 4
MB = HID // P
W_ORDER = (0, 2, 1, 3)
R = HID // P
GROUP = 64
CW = 512
CHUNKS = 2 * HID // CW
TOK = NB * P


def flamingo_layer(nc, x, ctx_in, g_xattn, g_ffn, w_turned, d_skip, w_gu, w_proj, out):
    ctx = ExitStack()
    with ctx:
        def sb(name, shape, dt):
            return ctx.enter_context(nc.sbuf_tensor(name, shape, dt))

        def sem(name):
            return ctx.enter_context(nc.semaphore(name))

        def view(buf, offset, *dims):
            row = 1
            for n in buf.shape[1:]:
                row *= n
            return bass.AP(tensor=buf, offset=offset, ap=[[row, P], *[list(d) for d in dims]])

        x_nat = sb("x_nat", [P, B, L], F32)
        c_nat = sb("c_nat", [P, B, L], F32)
        x1 = c_nat
        n_nat = sb("n_nat", [P, B, L], F32)
        toep = sb("toep", [P, H, L], F32)
        k_t = [sb(f"k_t{i}", [P, UNITS * WRAP], F32) for i in range(2)]
        q_t = [sb(f"q_t{i}", [P, UNITS * WRAP], F32) for i in range(2)]
        kv = [sb(f"kv{i}", [P, UNITS * PAIRS], F32) for i in range(2)]
        prod_a = sb("prod_a", [P, HU, ROWS_A, H * HD], F32)
        prod_b = sb("prod_b", [P, 2 * HG * HU * ROWS_B * WIDE], F32)
        fold_b = sb("fold_b", [P, HG * HU * WIDE], F32)
        sum_b = sb("sum_b", [P, HU, H * HD], F32)
        w_nat = sb("w_nat", [P, 2, R, L], BF16)
        wp_nat = sb("wp_nat", [P, LB, HID], BF16)
        wq = sb("wq", [P, LB, 2 * HID], BF16)
        wpq = sb("wpq", [P, R, L], BF16)
        w_abs = sb("w_abs", [P, CHUNKS, LB * CW], BF16)
        w_sgn = sb("w_sgn", [P, CHUNKS, LB * CW], BF16)
        w_scale = sb("w_scale", [P, CHUNKS, LB * CW], BF16)
        w_half = sb("w_half", [P, LB * CW], BF16)
        w_val = sb("w_val", [P, LB * CW], BF16)
        wp_abs = sb("wp_abs", [P, R, L], BF16)
        wp_sgn = sb("wp_sgn", [P, R, L], BF16)
        wp_scale = sb("wp_scale", [P, L], BF16)
        wp_half = sb("wp_half", [P, L], BF16)
        ident = sb("ident", [P, P], F32)
        ident_b = sb("ident_b", [P, P], BF16)
        anti = sb("anti", [P, P], F32)
        ones_col = sb("ones_col", [P, 2], F32)
        ones64 = sb("ones64", [P, P], BF16)
        ones8 = sb("ones8", [P, P], BF16)
        pick = sb("pick", [P, 2], BF16)
        d_row = sb("d_row", [P, H], F32)
        g_raw = sb("g_raw", [P, 2], F32)
        g_tanh = sb("g_tanh", [P, 2], F32)
        stats = sb("stats", [P, 4 * NB, 6], F32)
        mv = sb("mv", [P, 4 * NB, 2], F32)
        var_eps = sb("var_eps", [P, 4 * NB], F32)
        rstd = sb("rstd", [P, 4 * NB], F32)
        minus_half = sb("minus_half", [P, NB], F32)
        s_max = sb("s_max", [P, 4], F32)
        h_scale = sb("h_scale", [P, 4], F32)
        ms = sb("ms", [P, 2 * NB], F32)
        ms_r = sb("ms_r", [P, 2 * NB], F32)
        coef = sb("coef", [P, 2 * NB], F32)
        h_val = sb("h_val", [P, 2, TOK], F32)
        d_eye = kv[1][:, 0:HG * P].rearrange("p (h m) -> p h m", h=HG)
        xt = [k_t[i][:, 0:1024].bitcast(F16).rearrange("p (s d t) -> p s d t", s=2, d=LB) for i in range(2)]
        h_hi = kv[0][:, 0:2048].bitcast(F16).rearrange("p (m t) -> p m t", m=MB)
        h_lo = kv[0][:, 2048:4096].bitcast(F16).rearrange("p (m t) -> p m t", m=MB)
        silu = w_nat[:, 0].rearrange("p r l -> p (r l)").bitcast(F32).rearrange("p (n t) -> p n t", n=2)
        h_sq = w_nat[:, 1].rearrange("p r l -> p (r l)").bitcast(F32).rearrange("p (n t) -> p n t", n=2)
        h_acc = wp_nat[:, 0, :].bitcast(F32)

        ps = ctx.enter_context(nc.psum_tensor("ps", [P, 8, 512], F32))
        TP, YB, GU = 0, 2, 4

        ld_ctx = [sem(f"ld_ctx{i}") for i in range(2)]
        ld_x = [sem(f"ld_x{i}") for i in range(2)]
        ld_t = [sem(f"ld_t{g}") for g in range(H // HG)]
        ld_small = sem("ld_small")
        ld_w = [sem(f"ld_w{n}") for n in range(3)]
        ident_ready = sem("ident_ready")
        consts_ready = sem("consts_ready")
        sel_ready = sem("sel_ready")
        b_zeroed = sem("b_zeroed")
        pool_step = sem("pool_step")
        dve_step = sem("dve_step")
        diag_ready = sem("diag_ready")
        var_ready = sem("var_ready")
        rstd_ready = sem("rstd_ready")
        norm_ready = sem("norm_ready")
        tp_written = sem("tp_written")
        tp_read = sem("tp_read")
        k_ready = [sem(f"k_ready{i}") for i in range(2)]
        q_ready = [sem(f"q_ready{i}") for i in range(2)]
        kv_ready = [sem(f"kv_ready{i}") for i in range(2)]
        y_ready = sem("y_ready")
        y_used = sem("y_used")
        sumb_ready = sem("sumb_ready")
        sum_ready = sem("sum_ready")
        scale_ready = sem("scale_ready")
        clip_ready = sem("clip_ready")
        wq_ready = sem("wq_ready")
        wpq_ready = sem("wpq_ready")
        smax_psum = sem("smax_psum")
        smax_col = sem("smax_col")
        smax_all = sem("smax_all")
        hscale_ready = sem("hscale_ready")
        tanh_ready = sem("tanh_ready")
        red_ready = sem("red_ready")
        x1_ready = sem("x1_ready")
        xt_psum = sem("xt_psum")
        xhi_ready = sem("xhi_ready")
        xlo_ready = sem("xlo_ready")
        gate_ready = sem("gate_ready")
        up_ready = sem("up_ready")
        silu_ready = sem("silu_ready")
        h_ready = sem("h_ready")
        hhi_ready = sem("hhi_ready")
        hsq_ready = sem("hsq_ready")
        hacc_ready = sem("hacc_ready")
        hlo_ready = [sem(f"hlo_ready{i}") for i in range(2)]
        o_ready = sem("o_ready")
        ssq_ready = sem("ssq_ready")
        ms_ready = sem("ms_ready")
        coef_ready = sem("coef_ready")
        y_out = sem("y_out")
        stored = sem("stored")

        USE_K = (0, 6)
        USE_Q = (2, 8)
        USE_W = {0: 4, 2: 5, 1: 10, 3: 11}
        USE_WP = 12
        N_USES = USE_WP + 2
        ADDS = MB - 1

        def pair_products(eng, i, g):
            n = HG * HU
            k0, o0 = g * n * WRAP, g * n * PAIRS
            eng.tensor_tensor(view(kv[i], o0, (PAIRS, n), (HD, 4), (1, HD)),
                              view(k_t[i], k0, (WRAP, n), (0, 4), (1, HD)),
                              view(k_t[i], k0, (WRAP, n), (1, 4), (1, HD)), ALU.mult)
            eng.tensor_tensor(view(kv[i], o0 + 4 * HD, (PAIRS, n), (1, 4)),
                              view(k_t[i], k0, (WRAP, n), (1, 4)),
                              view(k_t[i], k0 + 4, (WRAP, n), (1, 4)), ALU.mult).then_inc(kv_ready[i], 1)

        def turned_x(i, part, n):
            return xt[i][:, part, :, 2 * P * n:2 * P * (n + 1)].rearrange("p d (b t) -> p b d t", b=2)

        def low_part(eng, i, m):
            n = MB * i + m
            eng.wait_ge(hhi_ready, n + 1)
            eng.tensor_tensor(h_lo[:, m, :], h_val[:, n % 2, :], h_hi[:, m, :], ALU.subtract)\
               .then_inc(hlo_ready[i], 1)

        block = ctx.enter_context(nc.Block())

        @block.sync
        def _(sp):
            def halves(t, i):
                return t[NB * i:NB * (i + 1)].rearrange("b p l -> p b l")

            def load_toeplitz(g):
                src = bass.AP(tensor=w_turned.tensor, offset=HG * g * (P + L), ap=[[1, P], [P + L, HG], [1, L]])
                sp.dma_start(toep[:, HG * g:HG * (g + 1), :], src).then_inc(ld_t[g], 16)

            sp.dma_start(c_nat[:, 0:NB, :], halves(ctx_in, 0)).then_inc(ld_ctx[0], 16)
            sp.dma_start(x_nat[:, 0:NB, :], halves(x, 0)).then_inc(ld_x[0], 16)
            load_toeplitz(0)
            load_toeplitz(1)
            load_toeplitz(2)
            load_toeplitz(3)
            sp.dma_start(c_nat[:, NB:B, :], halves(ctx_in, 1)).then_inc(ld_ctx[1], 16)
            sp.dma_start(x_nat[:, NB:B, :], halves(x, 1)).then_inc(ld_x[1], 16)
            for tb in range(B):
                sp.wait_ge(y_out, tb + 1)
                sp.dma_start(out[tb], x1[:, tb, :]).then_inc(stored, 16)
            sp.wait_ge(stored, 16 * B)

        @block.gpsimd
        def _(pool):
            steps = [0]

            def link(ins):
                steps[0] += 1
                ins.then_inc(pool_step, 1)
                pool.wait_ge(pool_step, steps[0])

            def inv_sqrt(k, n):
                pool.wait_ge(var_ready, n + 1)
                c = k if isinstance(k, slice) else slice(NB * k, NB * (k + 1))
                nc.gpsimd.tensor_tensor(rstd[:, c], var_eps[:, c], minus_half[:, 0:c.stop - c.start], ALU.pow)\
                    .then_inc(rstd_ready, 1)

            def diagonal(g):
                if g == 0:
                    pool.wait_ge(ld_small, 48)
                eye = view(anti, 0, (0, HG), (1, P))
                if g >= 1:
                    pool.wait_ge(diag_ready, g)
                link(nc.gpsimd.tensor_tensor(d_eye, eye, view(d_row, HG * g, (1, HG), (0, P)), ALU.mult))
                pool.wait_ge(ld_t[g], 16)
                t = toep[:, HG * g:HG * (g + 1), P:2 * P]
                nc.gpsimd.tensor_tensor(t, t, d_eye, ALU.add).then_inc(diag_ready, 1)

            def sum_rows_b(i, g):
                n = H // HG * i + g
                pool.wait_ge(y_used, HG * (n + 1))
                if i == 1 and g == 0:
                    pool.wait_ge(red_ready, NB)
                units = HG * HU
                row = [view(prod_b, n % 2 * units * ROWS_B * WIDE + r * WIDE, (ROWS_B * WIDE, units), (1, HD + 3))
                       for r in range(ROWS_B)]
                if n >= 1:
                    pool.wait_ge(sumb_ready, n)
                total = view(fold_b, 0, (WIDE, units), (1, HD + 3))
                link(nc.gpsimd.tensor_tensor(total, row[0], row[1], ALU.add))
                link(nc.gpsimd.tensor_tensor(total, total, row[2], ALU.add))
                nc.gpsimd.tensor_tensor(view(sum_b, HG * HD * g, (HD, HG), (H * HD, HU), (1, HD)),
                                        view(fold_b, 0, (HU * WIDE, HG), (WIDE, HU), (1, HD)),
                                        view(fold_b, HD, (HU * WIDE, HG), (WIDE, HU), (1, HD)),
                                        ALU.add).then_inc(sumb_ready, 1)

            def add_squares(i, m):
                n = MB * i + m
                pool.wait_ge(hsq_ready, n + 1)
                if i == 1 and m == 1:
                    pool.wait_ge(ssq_ready, 1)
                if m >= 2:
                    pool.wait_ge(hacc_ready, ADDS * i + m - 1)
                first = h_sq[:, 0, :] if m == 1 else h_acc
                nc.gpsimd.tensor_tensor(h_acc, first, h_sq[:, m % 2, :], ALU.add).then_inc(hacc_ready, 1)

            def coefs(i):
                pool.wait_ge(ms_ready, i + 1)
                if i == 0:
                    pool.wait_ge(tanh_ready, 1)
                c = slice(NB * i, NB * (i + 1))
                link(nc.gpsimd.tensor_tensor(ms_r[:, c], ms[:, c], minus_half[:], ALU.pow))
                nc.gpsimd.tensor_tensor(coef[:, c], ms_r[:, c], view(g_tanh, 1, (0, NB)), ALU.mult)\
                    .then_inc(coef_ready, 1)

            link(nc.gpsimd.memset(ident[:], 0.0))
            nc.gpsimd.affine_select(out=ident[:], in_=ident[:], compare_op=ALU.not_equal, fill=1.0, base=0,
                                    pattern=[[-1, P]], channel_multiplier=1).then_inc(ident_ready, 1)
            link(nc.gpsimd.memset(anti[:], 0.0))
            link(nc.gpsimd.affine_select(out=anti[:], in_=anti[:], compare_op=ALU.not_equal, fill=1.0, base=1 - P,
                                         pattern=[[1, P]], channel_multiplier=1))
            link(nc.gpsimd.memset(minus_half[:], -0.5))
            inv_sqrt(0, 0)
            diagonal(0)
            nc.gpsimd.memset(ones_col[:], 1.0)
            for n in range(2):
                pool.dma_start(w_nat[:, n, :, :], w_gu[HID * n:HID * (n + 1)].rearrange("(p r) l -> p r l", r=R))\
                    .then_inc(ld_w[n], 16)
            pool.dma_start(wp_nat[:], w_proj.rearrange("(t p) n -> p t n", p=P)).then_inc(ld_w[2], 16)
            nc.gpsimd.memset(fold_b[:], 0.0)
            nc.gpsimd.memset(prod_b[:], 0.0).then_inc(b_zeroed, 1)
            diagonal(1)
            diagonal(2)
            diagonal(3)
            link(nc.gpsimd.memset(ones8[:], 1.0))
            per = GROUP // R
            link(nc.gpsimd.affine_select(out=ones8[:], in_=ones8[:], compare_op=ALU.is_ge, fill=0.0, base=0,
                                         pattern=[[-per, P // per], [0, per]], channel_multiplier=1))
            nc.gpsimd.affine_select(out=ones8[:], in_=ones8[:], compare_op=ALU.is_ge, fill=0.0, base=per - 1,
                                    pattern=[[per, P // per], [0, per]],
                                    channel_multiplier=-1).then_inc(consts_ready, 1)
            inv_sqrt(1, 1)
            sum_rows_b(0, 0)
            pool.wait_ge(diag_ready, H // HG)
            pool.wait_ge(k_ready[1], 1)
            pair_products(nc.gpsimd, 1, 0)
            sum_rows_b(0, 1)
            pair_products(nc.gpsimd, 1, 1)
            sum_rows_b(0, 2)
            pair_products(nc.gpsimd, 1, 2)
            sum_rows_b(0, 3)
            pool.wait_ge(smax_col, 1)
            nc.gpsimd.partition_all_reduce(s_max[:, 1:2], s_max[:, 0:1], P, RMAX).then_inc(smax_all, 1)
            inv_sqrt(slice(2 * NB, 2 * NB + 2), 2)
            inv_sqrt(slice(2 * NB + 2, 3 * NB), 3)
            pair_products(nc.gpsimd, 1, 3)
            for m in range(MB):
                low_part(pool, 0, m)
                if m >= 1:
                    add_squares(0, m)
                if m % 2 == 1:
                    sum_rows_b(1, m // 2)
            inv_sqrt(slice(3 * NB, 3 * NB + 2), 4)
            inv_sqrt(slice(3 * NB + 2, 4 * NB), 5)
            coefs(0)
            for m in range(1, MB):
                add_squares(1, m)
            coefs(1)

        @block.scalar
        def _(act):
            act.dma_start(d_row[:], bass.AP(tensor=d_skip.tensor, offset=0, ap=[[0, P], [1, H]])).then_inc(ld_small, 16)
            for n, g in enumerate((g_xattn, g_ffn)):
                act.dma_start(g_raw[:, n:n + 1], bass.AP(tensor=g.tensor, offset=0, ap=[[0, P], [1, 1]]))\
                   .then_inc(ld_small, 16)
            act.wait_ge(ld_small, 48)
            nc.scalar.activation(g_tanh[:], g_raw[:], ACT.Tanh).then_inc(tanh_ready, 1)
            steps = [0]

            def evac_heads(dst, use, ready):
                for n in range(2):
                    act.wait_ge(tp_written, use + n + 1)
                    for lb in range(LB):
                        ins = nc.scalar.copy(
                            view(dst, lb * NB * WRAP + 2 * n * WRAP, (WRAP, 2), (HU * WRAP, H), (1, HD)),
                            view(ps, (TP + n) * 512 + lb * 256, (P, 2), (HD, H), (1, HD)))
                    ins.then_inc(tp_read, 1)
                act.wait_ge(tp_read, use + 2)
                nc.scalar.copy(view(dst, HD, (WRAP, UNITS), (1, 4)),
                               view(dst, 0, (WRAP, UNITS), (1, 4))).then_inc(ready, 1)

            def evac_w(use, a, s):
                act.wait_ge(tp_written, use + 1)
                bank = ps[:, TP + use % 2, :].bitcast(BF16)
                nc.scalar.activation(a, bank, ACT.Abs)
                nc.scalar.activation(s, bank, ACT.Sign).then_inc(tp_read, 1)

            def evac_scale(k):
                act.wait_ge(sum_ready, k + 1)
                bank = GU + 2 * (k % 2)
                nc.scalar.mul(w_scale[:, W_ORDER[k], :], view(ps, bank * 512, (1, LB * CW)), 1.0 / GROUP)\
                    .then_inc(scale_ready, 1)

            evac_heads(k_t[0], USE_K[0], k_ready[0])
            evac_heads(q_t[0], USE_Q[0], q_ready[0])
            for c in W_ORDER[:2]:
                evac_w(USE_W[c], w_abs[:, c, :], w_sgn[:, c, :])
            evac_scale(0)
            evac_scale(1)
            evac_heads(k_t[1], USE_K[1], k_ready[1])
            evac_heads(q_t[1], USE_Q[1], q_ready[1])
            for c in W_ORDER[2:]:
                evac_w(USE_W[c], w_abs[:, c, :], w_sgn[:, c, :])
            evac_scale(2)
            evac_scale(3)
            for n in range(2):
                r = slice(n * R // 2, (n + 1) * R // 2)
                evac_w(USE_WP + n, wp_abs[:, r, :], wp_sgn[:, r, :])
            act.wait_ge(sum_ready, CHUNKS + 1)
            nc.scalar.mul(wp_scale[:], ps[:, GU, 0:L], 1.0 / GROUP).then_inc(scale_ready, 1)

            def x_high(i):
                for n in range(2):
                    act.wait_ge(xt_psum, 2 * i + n + 1)
                    nc.scalar.copy(turned_x(i, 0, n), view(ps, (TP + n) * 512, (256, 2), (P, LB), (1, P)))\
                       .then_inc(xhi_ready, 1)

            def gate_silu(i, m):
                n = MB * i + m
                act.wait_ge(gate_ready, n + 1)
                if n >= 2:
                    act.wait_ge(h_ready, n - 1)
                nc.scalar.activation(silu[:, n % 2, :], ps[:, GU + 2 * (n % 2), :], ACT.Silu).then_inc(silu_ready, 1)

            def parts_of_h(i, m):
                n = MB * i + m
                act.wait_ge(h_ready, n + 1)
                if i == 1 and m == 0:
                    act.wait_ge(o_ready, NB)
                nc.scalar.copy(h_hi[:, m, :], h_val[:, n % 2, :]).then_inc(hhi_ready, 1)
                if m >= 2:
                    act.wait_ge(hacc_ready, ADDS * i + max(1, m - 2))
                elif i == 1:
                    act.wait_ge(hacc_ready, ADDS)
                nc.scalar.square(h_sq[:, m % 2, :], h_val[:, n % 2, :]).then_inc(hsq_ready, 1)

            for i in range(2):
                x_high(i)
                for m in range(MB + 1):
                    if m < MB:
                        gate_silu(i, m)
                    if m >= 1:
                        parts_of_h(i, m - 1)

        @block.vector
        def _(dve):
            steps = [0]

            def link(ins):
                steps[0] += 1
                ins.then_inc(dve_step, 1)
                dve.wait_ge(dve_step, steps[0])

            def norm_stats(src, k, i, bs):
                for b in bs:
                    last = nc.vector.bn_stats(stats[:, NB * k + b, :], src[:, NB * i + b, :])
                link(last)
                for b in bs:
                    last = nc.vector.bn_aggr(mv[:, NB * k + b, :], stats[:, NB * k + b, :])
                link(last)
                c = slice(NB * k + bs[0], NB * k + bs[-1] + 1)
                nc.vector.tensor_scalar(var_eps[:, c], mv[:, c, 1], LN_EPS, None, ALU.add).then_inc(var_ready, 1)

            def normalise(src, k, i, bs, turned):
                for b in bs:
                    o = (NB * i + b) * L
                    dst = view(n_nat, o + P - 1, (P, LB), (-1, P)) if turned else view(n_nat, o, (P, LB), (1, P))
                    nc.vector.tensor_scalar(dst, view(src, o, (P, LB), (1, P)), mv[:, NB * k + b, 0:1],
                                            rstd[:, NB * k + b:NB * k + b + 1],
                                            ALU.subtract, ALU.mult).then_inc(norm_ready, 1)

            def products(i, h):
                n = H * i + h
                dve.wait_ge(y_ready, n + 1)
                y0, q0 = (YB + n % 2) * 512, h * HU * WRAP
                a0, b0 = h * HD, h % (2 * HG) * HU * ROWS_B * WIDE
                if n >= 2 * HG and h % HG == 0:
                    dve.wait_ge(sumb_ready, n // HG - 1)
                if n == H:
                    dve.wait_ge(red_ready, NB)
                nc.vector.tensor_tensor(view(prod_a, a0, (ROWS_A * P, HU), (P, 4), (1, HD)),
                                        view(ps, y0, (PAIRS, HU), (HD, 4), (1, HD)),
                                        view(q_t[i], q0, (WRAP, HU), (1, 4), (1, HD)), ALU.mult)
                nc.vector.tensor_tensor(view(prod_a, a0 + 4 * P, (ROWS_A * P, HU), (4, 2), (1, 4)),
                                        view(ps, y0 + 4 * HD, (PAIRS, HU), (0, 2), (1, 4)),
                                        view(q_t[i], q0 + 4, (WRAP, HU), (4, 2), (1, 4)), ALU.mult)
                nc.vector.tensor_tensor(view(prod_b, b0 + 1, (ROWS_B * WIDE, HU), (WIDE + 1, ROWS_B), (1, HD)),
                                        view(ps, y0 + HD, (PAIRS, HU), (HD, ROWS_B), (1, HD)),
                                        view(q_t[i], q0, (WRAP, HU), (0, ROWS_B), (1, HD)),
                                        ALU.mult).then_inc(y_used, 1)

            def clip(k):
                s = w_scale[:, W_ORDER[k], :]
                dve.wait_ge(scale_ready, k + 1)
                nc.vector.tensor_scalar(s, s, 1e-8, None, ALU.max).then_inc(clip_ready, 1)

            def ternary(a, sgn, s, half, val, dst, done):
                nc.vector.tensor_scalar(half, s, 0.5, None, ALU.mult)
                link(nc.vector.tensor_tensor(val, s, a, ALU.subtract))
                link(nc.vector.tensor_tensor(val, a, val, ALU.add))
                link(nc.vector.tensor_tensor(a, a, half, ALU.is_gt))
                link(nc.vector.tensor_tensor(val, val, a, ALU.mult))
                nc.vector.tensor_tensor(dst, val, sgn, ALU.mult).then_inc(done, 1)

            def quantise(k):
                c = W_ORDER[k]
                dve.wait_ge(clip_ready, k + 1)
                dve.wait_ge(wq_ready, k) if k else None
                dst = wq[:, :, CW * c:CW * (c + 1)]
                pair = lambda t: t.rearrange("p (d j) -> p d j", d=LB)
                ternary(*(pair(t) for t in (w_abs[:, c, :], w_sgn[:, c, :], w_scale[:, c, :], w_half[:], w_val[:])),
                        dst, wq_ready)

            def quantise_projection():
                dve.wait_ge(scale_ready, CHUNKS + 1)
                link(nc.vector.tensor_scalar(wp_scale[:], wp_scale[:], 1e-8, None, ALU.max))
                link(nc.vector.tensor_scalar(wp_half[:], wp_scale[:], 0.5, None, ALU.mult))
                s, half = view(wp_scale, 0, (0, R), (1, L)), view(wp_half, 0, (0, R), (1, L))
                link(nc.vector.tensor_tensor(wpq[:], s, wp_abs[:], ALU.subtract))
                link(nc.vector.tensor_tensor(wpq[:], wp_abs[:], wpq[:], ALU.add))
                link(nc.vector.tensor_tensor(wp_abs[:], wp_abs[:], half, ALU.is_gt))
                link(nc.vector.tensor_tensor(wpq[:], wpq[:], wp_abs[:], ALU.mult))
                nc.vector.tensor_tensor(wpq[:], wpq[:], wp_sgn[:], ALU.mult).then_inc(wpq_ready, 1)

            def hidden_scale():
                dve.wait_ge(smax_psum, 1)
                nc.vector.tensor_reduce(s_max[:, 0:1], ps[:, GU + 3, 0:2 * LB * 2 * HID // P], AX.X, ALU.max)\
                    .then_inc(smax_col, 1)

            def hidden_scale_2():
                dve.wait_ge(smax_all, 1)
                link(nc.vector.reciprocal(s_max[:, 2:3], s_max[:, 1:2]))
                link(nc.vector.scalar_tensor_tensor(h_scale[:, 0:1], s_max[:, 2:3], 0.5, s_max[:, 2:3],
                                                    ALU.mult, ALU.mult))
                link(nc.vector.scalar_tensor_tensor(h_scale[:, 1:2], h_scale[:, 0:1], RMS_EPS, h_scale[:, 0:1],
                                                    ALU.mult, ALU.mult))

            def residual(i, b):
                if i == 0 and b == 0:
                    dve.wait_ge(tanh_ready, 1)
                dve.wait_ge(red_ready, NB * i + b + 1)
                o = (NB * i + b) * L
                nc.vector.scalar_tensor_tensor(
                    view(x1, o, (P, LB), (1, P)), view(ps, (GU + b) * 512 + P - 1, (P, LB), (-1, P)),
                    g_tanh[:, 0:1], view(x_nat, o, (P, LB), (1, P)), ALU.mult, ALU.add).then_inc(x1_ready, 1)

            def second_norm(i, between):
                for n in range(2):
                    bs = (2 * n, 2 * n + 1)
                    for b in bs:
                        residual(i, b)
                    dve.wait_ge(x1_ready, NB * i + bs[-1] + 1)
                    norm_stats(x1, 2 + i, i, bs)
                for n in range(2):
                    dve.wait_ge(rstd_ready, 3 + 2 * i + n)
                    normalise(x1, 2 + i, i, (2 * n, 2 * n + 1), False)
                    if n == 0:
                        between()

            def x_low(i):
                for n in range(2):
                    dve.wait_ge(xhi_ready, 2 * i + n + 1)
                    nc.vector.tensor_tensor(turned_x(i, 1, n),
                                            view(ps, (TP + n) * 512, (256, 2), (P, LB), (1, P)),
                                            turned_x(i, 0, n), ALU.subtract).then_inc(xlo_ready, 1)

            def hidden(i, m):
                n = MB * i + m
                dve.wait_ge(up_ready, n + 1)
                dve.wait_ge(silu_ready, n + 1)
                if n >= 2:
                    dve.wait_ge(hhi_ready, n - 1)
                    dve.wait_ge(hsq_ready, n - 1)
                    if m >= 2:
                        dve.wait_ge(hlo_ready[i], m - 1)
                    else:
                        dve.wait_ge(hlo_ready[0], MB - 1 + m)
                nc.vector.scalar_tensor_tensor(h_val[:, n % 2, :], ps[:, GU + 2 * (n % 2) + 1, :], h_scale[:, 0:1],
                                               silu[:, n % 2, :], ALU.mult, ALU.mult).then_inc(h_ready, 1)

            def mean_squares(i):
                dve.wait_ge(ssq_ready, i + 1)
                nc.vector.tensor_scalar(ms[:, NB * i:NB * (i + 1)], ps[:, YB, 0:NB], 1.0 / HID, h_scale[:, 1:2],
                                        ALU.mult, ALU.add).then_inc(ms_ready, 1)

            def result(i, b):
                tb = NB * i + b
                dve.wait_ge(coef_ready, i + 1)
                dve.wait_ge(o_ready, tb + 1)
                nc.vector.scalar_tensor_tensor(x1[:, tb, :], ps[:, TP + tb % 2, 0:L], coef[:, tb:tb + 1],
                                               x1[:, tb, :], ALU.mult, ALU.add).then_inc(y_out, 1)

            nc.vector.memset(pick[:], 0.0)
            link(nc.vector.memset(ones64[:], 0.0))
            for n in range(P // GROUP):
                g0 = GROUP * n
                nc.vector.memset(ones64[g0:g0 + GROUP, g0:g0 + GROUP], 1.0)
                nc.vector.memset(pick[g0:g0 + 1, n:n + 1], 1.0).then_inc(sel_ready, 1)
            dve.wait_ge(ident_ready, 1)
            nc.vector.tensor_copy(ident_b[:], ident[:]).then_inc(sel_ready, 1)
            half = tuple(range(NB))
            dve.wait_ge(ld_x[0], 16)
            norm_stats(x_nat, 0, 0, half)
            dve.wait_ge(k_ready[0], 1)
            pair_products(nc.vector, 0, 0)
            dve.wait_ge(rstd_ready, 1)
            normalise(x_nat, 0, 0, half, True)
            for g in range(1, H // HG):
                pair_products(nc.vector, 0, g)
            dve.wait_ge(q_ready[0], 1)
            dve.wait_ge(b_zeroed, 1)
            for h in range(H):
                products(0, h)
                if h == 3:
                    dve.wait_ge(ld_x[1], 16)
                    norm_stats(x_nat, 1, 1, half)
                if h == 5:
                    dve.wait_ge(rstd_ready, 2)
                    normalise(x_nat, 1, 1, half, True)
                if h == 7:
                    clip(0)
                if h == 8:
                    clip(1)
                    quantise(0)
                if h == 11:
                    quantise(1)
                if h == 13:
                    clip(2)
                if h == 14:
                    clip(3)
            hidden_scale()

            def first_of_second_half():
                hidden_scale_2()
                dve.wait_ge(q_ready[1], 1)
                products(1, 0)
                products(1, 1)

            second_norm(0, first_of_second_half)
            x_low(0)
            for m in range(MB):
                hidden(0, m)
                if m < MB - 1:
                    products(1, 2 * m + 2)
                    products(1, 2 * m + 3)
                if m < 2:
                    quantise(2 + m)
                if m == 3:
                    quantise_projection()
            second_norm(1, lambda: mean_squares(0))
            for b in range(NB):
                result(0, b)
            x_low(1)
            for m in range(MB):
                hidden(1, m)
                if m >= 1:
                    low_part(dve, 1, m - 1)
            low_part(dve, 1, MB - 1)
            mean_squares(1)
            for b in range(NB):
                result(1, b)

        @block.tensor
        def _(pe):
            def transpose(dst, src, start=True, stop=True):
                eye = ident if src.dtype == F32 else ident_b
                return nc.tensor.matmul(dst, src, eye[:], start=start, stop=stop, is_transpose=True)

            def tp_bank(use):
                if use >= 2:
                    pe.wait_ge(tp_read, use - 1)
                return TP + use % 2

            def heads(src, i, use):
                for n in range(2):
                    bank = tp_bank(use + n)
                    for lb in range(LB):
                        for b in range(2):
                            last = transpose(ps[:, bank, 256 * lb + P * b:256 * lb + P * (b + 1)],
                                             src[:, NB * i + 2 * n + b, P * lb:P * (lb + 1)])
                    last.then_inc(tp_written, 1)

            def ctx_heads(i):
                pe.wait_ge(ld_ctx[i], 16)
                heads(c_nat, i, USE_K[i])

            def q_heads(i):
                pe.wait_ge(norm_ready, NB * (i + 1))
                heads(n_nat, i, USE_Q[i])

            def conv(i, h):
                n = H * i + h
                if i == 0 and h % HG == 0:
                    pe.wait_ge(diag_ready, h // HG + 1)
                if h % HG == 0:
                    pe.wait_ge(kv_ready[i], h // HG + 1)
                if n >= 2:
                    pe.wait_ge(y_used, n - 1)
                o, w = h * HU * PAIRS, NB * PAIRS
                bank = YB + n % 2
                nc.tensor.matmul(ps[:, bank, 0:2 * w], toep[:, h, P:2 * P], kv[i][:, o:o + 2 * w], start=True, stop=False)
                nc.tensor.matmul(ps[:, bank, w:2 * w], toep[:, h, 0:P], kv[i][:, o:o + w],
                                 start=False, stop=True).then_inc(y_ready, 1)

            def w_transposes(c):
                half, r0 = c * CW // HID, (c * CW % HID) // P
                if c % 2 == 0:
                    pe.wait_ge(ld_w[half], 16)
                bank = ps[:, tp_bank(USE_W[c]), :].bitcast(BF16)
                for n in range(LB):
                    for r in range(CW // P):
                        o = CW * n + P * r
                        last = transpose(bank[:, o:o + P], w_nat[:, half, r0 + r, P * n:P * (n + 1)])
                last.then_inc(tp_written, 1)

            def group_sums(k):
                c = W_ORDER[k]
                pe.wait_ge(tp_read, USE_W[c] + 1)
                if k >= 2:
                    pe.wait_ge(scale_ready, k - 1)
                bank = GU + 2 * (k % 2)
                for n in range(LB):
                    last = nc.tensor.matmul(ps[:, bank + n, :], ones64[:], w_abs[:, c, CW * n:CW * (n + 1)],
                                            start=True, stop=True)
                last.then_inc(sum_ready, 1)

            def wp_transposes():
                pe.wait_ge(ld_w[2], 16)
                for n in range(2):
                    bank = ps[:, tp_bank(USE_WP + n), :].bitcast(BF16)
                    for r in range(R // 2 * n, R // 2 * (n + 1)):
                        for d in range(LB):
                            o = L * (r % (R // 2)) + P * d
                            last = transpose(bank[:, o:o + P], wp_nat[:, d, r::R])
                    last.then_inc(tp_written, 1)

            def wp_sums():
                pe.wait_ge(consts_ready, 1)
                pe.wait_ge(tp_read, N_USES)
                pe.wait_ge(scale_ready, CHUNKS)
                for r in range(R):
                    last = nc.tensor.matmul(ps[:, GU, 0:L], ones8[:], wp_abs[:, r, :], start=(r == 0), stop=(r == R - 1))
                last.then_inc(sum_ready, 1)

            def pick_scales():
                pe.wait_ge(clip_ready, CHUNKS)
                for c in range(CHUNKS):
                    for r in range(LB * CW // P):
                        o = 2 * (LB * CW // P * c + r)
                        last = nc.tensor.matmul(ps[:, GU + 3, o:o + 2], w_scale[:, c, P * r:P * (r + 1)],
                                                pick[:], start=True, stop=True)
                last.then_inc(smax_psum, 1)

            def reduce_rows(i):
                pe.wait_ge(y_used, H * (i + 1))
                pe.wait_ge(sumb_ready, H // HG * (i + 1))
                if i == 0:
                    pe.wait_ge(scale_ready, CHUNKS + 1)
                else:
                    pe.wait_ge(h_ready, MB)
                for b in range(NB):
                    if i == 0 and b == 3:
                        pe.wait_ge(smax_col, 1)
                    for lb in range(LB):
                        u = lb * NB + b
                        dst = ps[:, GU + b, P * lb:P * (lb + 1)]
                        for r in range(ROWS_A):
                            transpose(dst, prod_a[:, u, r, :], r == 0, False)
                        last = transpose(dst, sum_b[:, u, :], False, True)
                    last.then_inc(red_ready, 1)

            def x_transposes(i):
                if i == 0:
                    pe.wait_ge(tp_read, N_USES)
                else:
                    pe.wait_ge(y_out, NB)
                for n in range(2):
                    pe.wait_ge(norm_ready, NB * (2 + i) + 2 * n + 2)
                    for b in range(2):
                        for d in range(LB):
                            last = transpose(ps[:, TP + n, 256 * b + P * d:256 * b + P * (d + 1)],
                                             n_nat[:, NB * i + 2 * n + b, P * d:P * (d + 1)])
                    last.then_inc(xt_psum, 1)

            def gate_up(i, m):
                n = MB * i + m
                bank = GU + 2 * (n % 2)
                if m == 0:
                    pe.wait_ge(xlo_ready, 2 * i + 2)
                if n == 0:
                    pe.wait_ge(wq_ready, 2)
                if n == MB // 2:
                    pe.wait_ge(wq_ready, CHUNKS)
                if n >= 2:
                    pe.wait_ge(h_ready, n - 1)
                for half, ready in enumerate((gate_ready, up_ready)):
                    for d in range(LB):
                        for part in range(2):
                            last = nc.tensor.matmul(ps[:, bank + half, :],
                                                    wq[:, d, HID * half + P * m:HID * half + P * (m + 1)],
                                                    xt[i][:, part, d, :],
                                                    start=(d == 0 and part == 0), stop=(d == 1 and part == 1))
                    last.then_inc(ready, 1)

            def project(i, b):
                tb = NB * i + b
                bank = TP + tb % 2
                if b >= 2:
                    pe.wait_ge(y_out, tb - 1)
                elif b == 0:
                    pe.wait_ge(xlo_ready, 2 * i + 2)
                    pe.wait_ge(wpq_ready, 1)
                t = slice(P * b, P * (b + 1))
                for m in range(MB):
                    if b == 0:
                        pe.wait_ge(hhi_ready, MB * i + m + 1)
                    for part in range(2):
                        if b == 0 and part == 1:
                            pe.wait_ge(hlo_ready[i], m + 1)
                        last = nc.tensor.matmul(ps[:, bank, 0:L], (h_hi, h_lo)[part][:, m, t], wpq[:, m, :],
                                                start=(m == 0 and part == 0), stop=(m == MB - 1 and part == 1))
                last.then_inc(o_ready, 1)

            def sum_squares(i):
                pe.wait_ge(hacc_ready, ADDS * (i + 1))
                pe.wait_ge(y_used, 2 * H)
                for b in range(NB):
                    last = nc.tensor.matmul(ps[:, YB, b:b + 1], h_acc[:, P * b:P * (b + 1)], ones_col[:, 0:1],
                                            start=True, stop=True)
                last.then_inc(ssq_ready, 1)

            pe.wait_ge(ident_ready, 1)
            ctx_heads(0)
            conv(0, 0)
            conv(0, 1)
            q_heads(0)
            for h in range(2, H):
                conv(0, h)
                if h == 3:
                    pe.wait_ge(sel_ready, 3)
                    w_transposes(W_ORDER[0])
                if h == 4:
                    w_transposes(W_ORDER[1])
                if h == 5:
                    group_sums(0)
                if h == 6:
                    group_sums(1)
                    ctx_heads(1)
                if h == 8:
                    q_heads(1)
                if h == 9:
                    w_transposes(W_ORDER[2])
                if h == 10:
                    w_transposes(W_ORDER[3])
                if h == 11:
                    group_sums(2)
                if h == 12:
                    group_sums(3)
                if h == 13:
                    wp_transposes()
            wp_sums()
            pick_scales()
            reduce_rows(0)
            conv(1, 0)
            conv(1, 1)
            x_transposes(0)
            for m in range(MB):
                gate_up(0, m)
                if m < MB - 1:
                    conv(1, 2 * m + 2)
                    conv(1, 2 * m + 3)
            project(0, 0)
            reduce_rows(1)
            sum_squares(0)
            project(0, 1)
            project(0, 2)
            project(0, 3)
            x_transposes(1)
            for m in range(MB):
                gate_up(1, m)
            project(1, 0)
            sum_squares(1)
            for b in range(1, NB):
                project(1, b)


def kernel(x, ctx_2048, g_xattn, g_ffn, L0_xattn_ssm_kernel, L0_xattn_D, L0_ffn_w_gate_up, L0_ffn_w_proj):
    import numpy as np
    import concourse.bacc as bacc
    from concourse.bass_utils import run_bass_kernel_spmd

    nc = bacc.Bacc("TRN2", target_bir_lowering=False, num_devices=1)
    turned = np.zeros((H, P + L), np.float32)
    turned[:, :L] = np.asarray(L0_xattn_ssm_kernel)[:, ::-1]
    arrays = {
        "x": x, "ctx_in": ctx_2048, "g_xattn": g_xattn, "g_ffn": g_ffn, "w_turned": turned,
        "d_skip": L0_xattn_D, "w_gu": L0_ffn_w_gate_up, "w_proj": L0_ffn_w_proj,
    }
    arrays = {name: np.ascontiguousarray(a) for name, a in arrays.items()}
    args = [nc.dram_tensor(name, a.shape, mybir.dt.from_np(a.dtype), kind="ExternalInput").ap()
            for name, a in arrays.items()]
    out = nc.dram_tensor("out", (B, D_MODEL, L), F32, kind="ExternalOutput").ap()
    flamingo_layer(nc, *args, out)
    return run_bass_kernel_spmd(nc, [arrays], core_ids=[0]).results[0]["out"]
```

```python
from contextlib import ExitStack

import concourse.bass as bass
from concourse import mybir

ALU = mybir.AluOpType
ACT = mybir.ActivationFunctionType
AX = mybir.AxisListType
F32 = mybir.dt.float32
F16 = mybir.dt.float16
BF16 = mybir.dt.bfloat16
RMAX = bass.bass_isa.ReduceOp.max

P = 128
B, D_MODEL, L = 8, 128, 256
H, HD = 16, 8
HID = 1024
LN_EPS = 1e-5
RMS_EPS = 2.0 ** -23
NB = 4
LB = L // P
UNITS = H * LB * NB
HU = LB * NB
WRAP = 12
PAIRS = 36
ROWS_A, ROWS_B = 5, 3
WIDE = 16
HG = 4
MB = HID // P
W_ORDER = (0, 2, 1, 3)
R = HID // P
GROUP = 64
CW = 512
CHUNKS = 2 * HID // CW
TOK = NB * P


def flamingo_layer(nc, x, ctx_in, g_xattn, g_ffn, w_turned, d_skip, w_gu, w_proj, out):
    ctx = ExitStack()
    with ctx:
        def sb(name, shape, dt):
            return ctx.enter_context(nc.sbuf_tensor(name, shape, dt))

        def sem(name):
            return ctx.enter_context(nc.semaphore(name))

        def view(buf, offset, *dims):
            row = 1
            for n in buf.shape[1:]:
                row *= n
            return bass.AP(tensor=buf, offset=offset, ap=[[row, P], *[list(d) for d in dims]])

        x_nat = sb("x_nat", [P, B, L], F32)
        c_nat = sb("c_nat", [P, B, L], F32)
        x1 = c_nat
        n_nat = sb("n_nat", [P, B, L], F32)
        toep = sb("toep", [P, H, L], F32)
        k_t = [sb(f"k_t{i}", [P, UNITS * WRAP], F32) for i in range(2)]
        q_t = [sb(f"q_t{i}", [P, UNITS * WRAP], F32) for i in range(2)]
        kv = [sb(f"kv{i}", [P, UNITS * PAIRS], F32) for i in range(2)]
        prod_a = sb("prod_a", [P, HU, ROWS_A, H * HD], F32)
        prod_b = sb("prod_b", [P, 2 * HG * HU * ROWS_B * WIDE], F32)
        fold_b = sb("fold_b", [P, HG * HU * WIDE], F32)
        sum_b = sb("sum_b", [P, HU, H * HD], F32)
        w_nat = sb("w_nat", [P, 2, R, L], BF16)
        wp_nat = sb("wp_nat", [P, LB, HID], BF16)
        wq = sb("wq", [P, LB, 2 * HID], BF16)
        wpq = sb("wpq", [P, R, L], BF16)
        w_abs = sb("w_abs", [P, CHUNKS, LB * CW], BF16)
        w_sgn = sb("w_sgn", [P, CHUNKS, LB * CW], BF16)
        w_scale = sb("w_scale", [P, CHUNKS, LB * CW], BF16)
        w_half = sb("w_half", [P, LB * CW], BF16)
        w_val = sb("w_val", [P, 2, LB * CW], BF16)
        wp_abs = sb("wp_abs", [P, R, L], BF16)
        wp_sgn = sb("wp_sgn", [P, R, L], BF16)
        wp_scale = sb("wp_scale", [P, L], BF16)
        wp_half = sb("wp_half", [P, L], BF16)
        ident = sb("ident", [P, P], F32)
        ident_b = sb("ident_b", [P, P], BF16)
        anti = sb("anti", [P, P], F32)
        ones_col = sb("ones_col", [P, 2], F32)
        ones64 = sb("ones64", [P, P], BF16)
        ones8 = sb("ones8", [P, P], BF16)
        pick = sb("pick", [P, 2], BF16)
        d_row = sb("d_row", [P, H], F32)
        g_raw = sb("g_raw", [P, 2], F32)
        g_tanh = sb("g_tanh", [P, 2], F32)
        stats = sb("stats", [P, 4 * NB, 6], F32)
        mv = sb("mv", [P, 4 * NB, 2], F32)
        var_eps = sb("var_eps", [P, 4 * NB], F32)
        rstd = sb("rstd", [P, 4 * NB], F32)
        minus_half = sb("minus_half", [P, NB], F32)
        s_max = sb("s_max", [P, 4], F32)
        h_scale = sb("h_scale", [P, 4], F32)
        ms = sb("ms", [P, 2 * NB], F32)
        ms_r = sb("ms_r", [P, 2 * NB], F32)
        coef = sb("coef", [P, 2 * NB], F32)
        d_eye = kv[1][:, 0:H * P].rearrange("p (h m) -> p h m", h=H)
        xt = [k_t[i][:, 0:1024].bitcast(F16).rearrange("p (s d t) -> p s d t", s=2, d=LB) for i in range(2)]
        h_hi = kv[0][:, 0:2048].bitcast(F16).rearrange("p (m t) -> p m t", m=MB)
        h_lo = kv[0][:, 2048:4096].bitcast(F16).rearrange("p (m t) -> p m t", m=MB)
        silu = w_nat[:, 0].rearrange("p r l -> p (r l)").bitcast(F32).rearrange("p (n t) -> p n t", n=2)
        h_val = [w_nat[:, 1].rearrange("p r l -> p (r l)").bitcast(F32)[:, TOK * n:TOK * (n + 1)] for n in range(2)]
        h_val.append(k_t[0][:, 2 * TOK:3 * TOK])
        h_sq = [q_t[0][:, TOK * n:TOK * (n + 1)] for n in range(3)]
        h_sq.append(k_t[1][:, 2 * TOK:3 * TOK])
        h_sq += [t[:, b:b + 2, :].rearrange("p b l -> p (b l)") for t in (x_nat, n_nat) for b in (0, 2)]
        h_acc = wp_nat[:, 0, :].bitcast(F32)

        ps = ctx.enter_context(nc.psum_tensor("ps", [P, 8, 512], F32))
        TP, YB, GU, XT = 0, 2, 4, 6
        WPS, PICK = GU + 2, GU + 3
        OUT = (TP, TP + 1, YB, YB + 1)

        ld_ctx = [sem(f"ld_ctx{i}") for i in range(2)]
        ld_x = [sem(f"ld_x{i}") for i in range(2)]
        ld_t = [sem(f"ld_t{g}") for g in range(H // HG)]
        ld_d = sem("ld_d")
        ld_g = sem("ld_g")
        ld_w = [sem(f"ld_w{n}") for n in range(3)]
        ident_ready = sem("ident_ready")
        consts_ready = sem("consts_ready")
        sel_ready = sem("sel_ready")
        pool_step = sem("pool_step")
        dve_step = sem("dve_step")
        deye_ready = sem("deye_ready")
        diag_ready = sem("diag_ready")
        var_ready = sem("var_ready")
        rstd_ready = sem("rstd_ready")
        norm_ready = sem("norm_ready")
        tp_written = sem("tp_written")
        tp_read = sem("tp_read")
        k_ready = [sem(f"k_ready{i}") for i in range(2)]
        q_ready = [sem(f"q_ready{i}") for i in range(2)]
        kv_ready = [sem(f"kv_ready{i}") for i in range(2)]
        kv_first = sem("kv_first")
        y_ready = sem("y_ready")
        y_used = sem("y_used")
        sumb_ready = sem("sumb_ready")
        sum_ready = sem("sum_ready")
        scale_ready = sem("scale_ready")
        clip_ready = sem("clip_ready")
        val_ready = sem("val_ready")
        wq_ready = sem("wq_ready")
        wp_step = sem("wp_step")
        wpq_ready = sem("wpq_ready")
        smax_psum = sem("smax_psum")
        smax_col = sem("smax_col")
        smax_all = sem("smax_all")
        hscale_ready = sem("hscale_ready")
        tanh_ready = sem("tanh_ready")
        red_ready = sem("red_ready")
        x1_ready = sem("x1_ready")
        xt_psum = sem("xt_psum")
        xhi_ready = sem("xhi_ready")
        xlo_ready = sem("xlo_ready")
        gate_ready = sem("gate_ready")
        up_ready = sem("up_ready")
        silu_ready = sem("silu_ready")
        h_ready = sem("h_ready")
        hhi_ready = sem("hhi_ready")
        hsq_ready = sem("hsq_ready")
        hacc_ready = sem("hacc_ready")
        hlo_ready = [sem(f"hlo_ready{i}") for i in range(2)]
        o_ready = sem("o_ready")
        ssq_ready = sem("ssq_ready")
        ms_ready = sem("ms_ready")
        coef_ready = sem("coef_ready")
        y_out = sem("y_out")
        stored = sem("stored")

        USE_K = (0, 6)
        USE_Q = (2, 12)
        USE_W = {0: 4, 2: 5, 1: 8, 3: 9}
        USE_WP = 10
        ADDS = MB - 1
        Q_STEPS = (1, 1, 1, 2)
        WP_STEPS = 6
        POOL_VALUES = (0, 1, 3)

        def pair_products(eng, i, g):
            n = HG * HU
            k0, o0 = g * n * WRAP, g * n * PAIRS
            eng.tensor_tensor(view(kv[i], o0, (PAIRS, n), (HD, 4), (1, HD)),
                              view(k_t[i], k0, (WRAP, n), (0, 4), (1, HD)),
                              view(k_t[i], k0, (WRAP, n), (1, 4), (1, HD)), ALU.mult)
            eng.tensor_tensor(view(kv[i], o0 + 4 * HD, (PAIRS, n), (1, 4)),
                              view(k_t[i], k0, (WRAP, n), (1, 4)),
                              view(k_t[i], k0 + 4, (WRAP, n), (1, 4)), ALU.mult)\
               .then_inc(kv_first if i == 0 and g < 3 else kv_ready[i], 1)

        def turned_x(i, part, n):
            return xt[i][:, part, :, 2 * P * n:2 * P * (n + 1)].rearrange("p d (b t) -> p b d t", b=2)

        def low_part(eng, i, m):
            n = MB * i + m
            eng.wait_ge(hhi_ready, n + 1)
            eng.tensor_tensor(h_lo[:, m, :], h_val[n % len(h_val)], h_hi[:, m, :], ALU.subtract)\
               .then_inc(hlo_ready[i], 1)

        block = ctx.enter_context(nc.Block())

        @block.sync
        def _(sp):
            def halves(t, i):
                return t[NB * i:NB * (i + 1)].rearrange("b p l -> p b l")

            def load_toeplitz(g):
                src = bass.AP(tensor=w_turned.tensor, offset=HG * g * (P + L), ap=[[1, P], [P + L, HG], [1, L]])
                sp.dma_start(toep[:, HG * g:HG * (g + 1), :], src).then_inc(ld_t[g], 16)

            sp.dma_start(x_nat[:, 0:NB, :], halves(x, 0)).then_inc(ld_x[0], 16)
            sp.dma_start(c_nat[:, 0:NB, :], halves(ctx_in, 0)).then_inc(ld_ctx[0], 16)
            load_toeplitz(0)
            load_toeplitz(1)
            load_toeplitz(2)
            load_toeplitz(3)
            sp.dma_start(x_nat[:, NB:B, :], halves(x, 1)).then_inc(ld_x[1], 16)
            sp.dma_start(c_nat[:, NB:B, :], halves(ctx_in, 1)).then_inc(ld_ctx[1], 16)
            for tb in range(B):
                sp.wait_ge(y_out, tb + 1)
                sp.dma_start(out[tb], x1[:, tb, :]).then_inc(stored, 16)
            sp.wait_ge(stored, 16 * B)

        @block.gpsimd
        def _(pool):
            steps = [0]

            def link(ins):
                steps[0] += 1
                ins.then_inc(pool_step, 1)
                pool.wait_ge(pool_step, steps[0])

            def inv_sqrt(k, n):
                pool.wait_ge(var_ready, n + 1)
                c = k if isinstance(k, slice) else slice(NB * k, NB * (k + 1))
                nc.gpsimd.tensor_tensor(rstd[:, c], var_eps[:, c], minus_half[:, 0:c.stop - c.start], ALU.pow)\
                    .then_inc(rstd_ready, 1)

            def d_on_diagonal(g):
                nc.gpsimd.tensor_tensor(d_eye[:, HG * g:HG * (g + 1), :], view(anti, 0, (0, HG), (1, P)),
                                        view(d_row, HG * g, (1, HG), (0, P)), ALU.mult).then_inc(deye_ready, 1)

            def diagonal(g):
                h = slice(HG * g, HG * (g + 1))
                pool.wait_ge(deye_ready, g + 1)
                pool.wait_ge(ld_t[g], 16)
                nc.gpsimd.tensor_tensor(toep[:, h, P:2 * P], toep[:, h, P:2 * P], d_eye[:, h, :], ALU.add)\
                    .then_inc(diag_ready, 1)

            def sum_rows_b(i, g):
                n = H // HG * i + g
                pool.wait_ge(y_used, HG * (n + 1))
                if i == 1 and g == 0:
                    pool.wait_ge(red_ready, NB)
                units = HG * HU
                row = [view(prod_b, n % 2 * units * ROWS_B * WIDE + r * WIDE, (ROWS_B * WIDE, units), (1, HD + 3))
                       for r in range(ROWS_B)]
                if n >= 1:
                    pool.wait_ge(sumb_ready, n)
                total = view(fold_b, 0, (WIDE, units), (1, HD + 3))
                link(nc.gpsimd.tensor_tensor(total, row[0], row[1], ALU.add))
                link(nc.gpsimd.tensor_tensor(total, total, row[2], ALU.add))
                nc.gpsimd.tensor_tensor(view(sum_b, HG * HD * g, (HD, HG), (H * HD, HU), (1, HD)),
                                        view(fold_b, 0, (HU * WIDE, HG), (WIDE, HU), (1, HD)),
                                        view(fold_b, HD, (HU * WIDE, HG), (WIDE, HU), (1, HD)),
                                        ALU.add).then_inc(sumb_ready, 1)

            def values(k):
                s, a, val = w_scale[:, W_ORDER[k], :], w_abs[:, W_ORDER[k], :], w_val[:, k % 2, :]
                pool.wait_ge(clip_ready, k + 1)
                if k >= 2:
                    pool.wait_ge(wq_ready, sum(Q_STEPS[:k - 1]))
                link(nc.gpsimd.tensor_tensor(val, s, a, ALU.subtract))
                nc.gpsimd.tensor_tensor(val, a, val, ALU.add).then_inc(val_ready, 1)

            def add_squares(i, m):
                n = MB * i + m
                pool.wait_ge(hsq_ready, n + 1)
                if i == 1 and m == 1:
                    pool.wait_ge(ssq_ready, 1)
                if m >= 2:
                    pool.wait_ge(hacc_ready, ADDS * i + m - 1)
                first = h_sq[(n - 1) % len(h_sq)] if m == 1 else h_acc
                nc.gpsimd.tensor_tensor(h_acc, first, h_sq[n % len(h_sq)], ALU.add).then_inc(hacc_ready, 1)

            def coefs(i):
                pool.wait_ge(ms_ready, i + 1)
                if i == 0:
                    pool.wait_ge(tanh_ready, 1)
                c = slice(NB * i, NB * (i + 1))
                link(nc.gpsimd.tensor_tensor(ms_r[:, c], ms[:, c], minus_half[:], ALU.pow))
                nc.gpsimd.tensor_tensor(coef[:, c], ms_r[:, c], view(g_tanh, 1, (0, NB)), ALU.mult)\
                    .then_inc(coef_ready, 1)

            link(nc.gpsimd.memset(ident[:], 0.0))
            nc.gpsimd.affine_select(out=ident[:], in_=ident[:], compare_op=ALU.not_equal, fill=1.0, base=0,
                                    pattern=[[-1, P]], channel_multiplier=1).then_inc(ident_ready, 1)
            link(nc.gpsimd.memset(anti[:], 0.0))
            link(nc.gpsimd.affine_select(out=anti[:], in_=anti[:], compare_op=ALU.not_equal, fill=1.0, base=1 - P,
                                         pattern=[[1, P]], channel_multiplier=1))
            link(nc.gpsimd.memset(minus_half[:], -0.5))
            for n in range(2):
                pool.dma_start(w_nat[:, n, :, :], w_gu[HID * n:HID * (n + 1)].rearrange("(p r) l -> p r l", r=R))\
                    .then_inc(ld_w[n], 16)
            pool.dma_start(wp_nat[:], w_proj.rearrange("(t p) n -> p t n", p=P)).then_inc(ld_w[2], 16)
            pool.wait_ge(ld_d, 16)
            d_on_diagonal(0)
            inv_sqrt(0, 0)
            diagonal(0)
            d_on_diagonal(1)
            diagonal(1)
            d_on_diagonal(2)
            diagonal(2)
            d_on_diagonal(3)
            diagonal(3)
            pool.wait_ge(k_ready[0], 1)
            pair_products(nc.gpsimd, 0, 3)
            link(nc.gpsimd.memset(ones8[:], 1.0))
            per = GROUP // R
            link(nc.gpsimd.affine_select(out=ones8[:], in_=ones8[:], compare_op=ALU.is_ge, fill=0.0, base=0,
                                         pattern=[[-per, P // per], [0, per]], channel_multiplier=1))
            nc.gpsimd.affine_select(out=ones8[:], in_=ones8[:], compare_op=ALU.is_ge, fill=0.0, base=per - 1,
                                    pattern=[[per, P // per], [0, per]],
                                    channel_multiplier=-1).then_inc(consts_ready, 1)
            sum_rows_b(0, 0)
            pool.wait_ge(diag_ready, H // HG)
            pool.wait_ge(k_ready[1], 1)
            inv_sqrt(1, 1)
            sum_rows_b(0, 1)
            values(POOL_VALUES[0])
            values(POOL_VALUES[1])
            sum_rows_b(0, 2)
            sum_rows_b(0, 3)
            pair_products(nc.gpsimd, 1, 0)
            pair_products(nc.gpsimd, 1, 1)
            inv_sqrt(slice(2 * NB, 2 * NB + 2), 2)
            inv_sqrt(slice(2 * NB + 2, 3 * NB), 3)
            pool.wait_ge(smax_col, 1)
            nc.gpsimd.partition_all_reduce(s_max[:, 1:2], s_max[:, 0:1], P, RMAX).then_inc(smax_all, 1)
            values(POOL_VALUES[2])
            pair_products(nc.gpsimd, 1, 2)
            pair_products(nc.gpsimd, 1, 3)
            for m in range(MB):
                if m % 2 == 1:
                    sum_rows_b(1, m // 2)
                low_part(pool, 0, m)
            add_squares(0, 1)
            add_squares(0, 2)
            inv_sqrt(slice(3 * NB, 3 * NB + 2), 4)
            add_squares(0, 3)
            inv_sqrt(slice(3 * NB + 2, 4 * NB), 5)
            for m in range(4, MB):
                add_squares(0, m)
            coefs(0)
            for m in range(1, MB):
                add_squares(1, m)
            coefs(1)

        @block.scalar
        def _(act):
            act.dma_start(d_row[:], bass.AP(tensor=d_skip.tensor, offset=0, ap=[[0, P], [1, H]])).then_inc(ld_d, 16)
            for n, g in enumerate((g_xattn, g_ffn)):
                act.dma_start(g_raw[:, n:n + 1], bass.AP(tensor=g.tensor, offset=0, ap=[[0, P], [1, 1]]))\
                   .then_inc(ld_g, 16)
            steps = [0]

            def evac_heads(dst, use, ready):
                for n in range(2):
                    act.wait_ge(tp_written, use + n + 1)
                    for lb in range(LB):
                        ins = nc.scalar.copy(
                            view(dst, lb * NB * WRAP + 2 * n * WRAP, (WRAP, 2), (HU * WRAP, H), (1, HD)),
                            view(ps, (TP + n) * 512 + lb * 256, (P, 2), (HD, H), (1, HD)))
                    ins.then_inc(tp_read, 1)
                act.wait_ge(tp_read, use + 2)
                nc.scalar.copy(view(dst, HD, (WRAP, UNITS), (1, 4)),
                               view(dst, 0, (WRAP, UNITS), (1, 4))).then_inc(ready, 1)

            def evac_w(use, a, s):
                act.wait_ge(tp_written, use + 1)
                bank = ps[:, TP + use % 2, :].bitcast(BF16)
                nc.scalar.activation(a, bank, ACT.Abs)
                nc.scalar.activation(s, bank, ACT.Sign).then_inc(tp_read, 1)

            def evac_scale(k):
                act.wait_ge(sum_ready, k + 1)
                bank = GU + 2 * (k % 2)
                nc.scalar.mul(w_scale[:, W_ORDER[k], :], view(ps, bank * 512, (1, LB * CW)), 1.0 / GROUP)\
                    .then_inc(scale_ready, 1)

            evac_heads(k_t[0], USE_K[0], k_ready[0])
            act.wait_ge(ld_g, 32)
            nc.scalar.activation(g_tanh[:], g_raw[:], ACT.Tanh).then_inc(tanh_ready, 1)
            evac_heads(q_t[0], USE_Q[0], q_ready[0])
            for c in W_ORDER[:2]:
                evac_w(USE_W[c], w_abs[:, c, :], w_sgn[:, c, :])
            evac_scale(0)
            evac_scale(1)
            evac_heads(k_t[1], USE_K[1], k_ready[1])
            for c in W_ORDER[2:]:
                evac_w(USE_W[c], w_abs[:, c, :], w_sgn[:, c, :])
            evac_scale(2)
            evac_scale(3)
            for n in range(2):
                r = slice(n * R // 2, (n + 1) * R // 2)
                evac_w(USE_WP + n, wp_abs[:, r, :], wp_sgn[:, r, :])
            act.wait_ge(sum_ready, CHUNKS + 1)
            nc.scalar.mul(wp_scale[:], ps[:, WPS, 0:L], 1.0 / GROUP).then_inc(scale_ready, 1)
            evac_heads(q_t[1], USE_Q[1], q_ready[1])

            def x_high(i):
                for n in range(2):
                    act.wait_ge(xt_psum, 2 * i + n + 1)
                    nc.scalar.copy(turned_x(i, 0, n), view(ps, (XT + n) * 512, (256, 2), (P, LB), (1, P)))\
                       .then_inc(xhi_ready, 1)

            def gate_silu(i, m):
                n = MB * i + m
                act.wait_ge(gate_ready, n + 1)
                if n >= 2:
                    act.wait_ge(h_ready, n - 1)
                nc.scalar.activation(silu[:, n % 2, :], ps[:, GU + 2 * (n % 2), :], ACT.Silu).then_inc(silu_ready, 1)

            def parts_of_h(i, m):
                n = MB * i + m
                act.wait_ge(h_ready, n + 1)
                if i == 1 and m == 0:
                    act.wait_ge(o_ready, NB)
                nc.scalar.copy(h_hi[:, m, :], h_val[n % len(h_val)]).then_inc(hhi_ready, 1)
                if n >= len(h_sq):
                    last = n - len(h_sq)
                    act.wait_ge(hacc_ready, ADDS * (last // MB) + max(1, last % MB))
                nc.scalar.square(h_sq[n % len(h_sq)], h_val[n % len(h_val)]).then_inc(hsq_ready, 1)

            for i in range(2):
                x_high(i)
                for m in range(MB + 1):
                    if m < MB:
                        gate_silu(i, m)
                    if m >= 1:
                        parts_of_h(i, m - 1)

        @block.vector
        def _(dve):
            steps = [0]

            def link(ins):
                steps[0] += 1
                ins.then_inc(dve_step, 1)
                dve.wait_ge(dve_step, steps[0])

            def norm_stats(src, k, i, bs):
                for b in bs:
                    last = nc.vector.bn_stats(stats[:, NB * k + b, :], src[:, NB * i + b, :])
                link(last)
                for b in bs:
                    last = nc.vector.bn_aggr(mv[:, NB * k + b, :], stats[:, NB * k + b, :])
                link(last)
                c = slice(NB * k + bs[0], NB * k + bs[-1] + 1)
                nc.vector.tensor_scalar(var_eps[:, c], mv[:, c, 1], LN_EPS, None, ALU.add).then_inc(var_ready, 1)

            def normalise(src, k, i, bs, turned):
                for b in bs:
                    o = (NB * i + b) * L
                    dst = view(n_nat, o + P - 1, (P, LB), (-1, P)) if turned else view(n_nat, o, (P, LB), (1, P))
                    nc.vector.tensor_scalar(dst, view(src, o, (P, LB), (1, P)), mv[:, NB * k + b, 0:1],
                                            rstd[:, NB * k + b:NB * k + b + 1],
                                            ALU.subtract, ALU.mult).then_inc(norm_ready, 1)

            def products(i, h):
                n = H * i + h
                dve.wait_ge(y_ready, n + 1)
                y0, q0 = (YB + n % 2) * 512, h * HU * WRAP
                a0, b0 = h * HD, h % (2 * HG) * HU * ROWS_B * WIDE
                if n >= 2 * HG and h % HG == 0:
                    dve.wait_ge(sumb_ready, n // HG - 1)
                if n == H:
                    dve.wait_ge(red_ready, NB)
                nc.vector.tensor_tensor(view(prod_a, a0, (ROWS_A * P, HU), (P, 4), (1, HD)),
                                        view(ps, y0, (PAIRS, HU), (HD, 4), (1, HD)),
                                        view(q_t[i], q0, (WRAP, HU), (1, 4), (1, HD)), ALU.mult)
                nc.vector.tensor_tensor(view(prod_a, a0 + 4 * P, (ROWS_A * P, HU), (4, 2), (1, 4)),
                                        view(ps, y0 + 4 * HD, (PAIRS, HU), (0, 2), (1, 4)),
                                        view(q_t[i], q0 + 4, (WRAP, HU), (4, 2), (1, 4)), ALU.mult)
                nc.vector.tensor_tensor(view(prod_b, b0 + 1, (ROWS_B * WIDE, HU), (WIDE + 1, ROWS_B), (1, HD)),
                                        view(ps, y0 + HD, (PAIRS, HU), (HD, ROWS_B), (1, HD)),
                                        view(q_t[i], q0, (WRAP, HU), (0, ROWS_B), (1, HD)),
                                        ALU.mult).then_inc(y_used, 1)

            def clip(k):
                s = w_scale[:, W_ORDER[k], :]
                dve.wait_ge(scale_ready, k + 1)
                nc.vector.tensor_scalar(s, s, 1e-8, None, ALU.max).then_inc(clip_ready, 1)

            def quantise(k, n=0):
                c, size = W_ORDER[k], LB // Q_STEPS[k]
                if k not in POOL_VALUES:
                    dve.wait_ge(clip_ready, k + 1)
                elif n == 0:
                    dve.wait_ge(val_ready, POOL_VALUES.index(k) + 1)
                if k:
                    dve.wait_ge(wq_ready, sum(Q_STEPS[:k]) + n)
                j = slice(CW * size * n, CW * size * (n + 1))
                a, sgn, s, val, half = (t.rearrange("p (d j) -> p d j", d=size) for t in (
                    w_abs[:, c, j], w_sgn[:, c, j], w_scale[:, c, j], w_val[:, k % 2, j], w_half[:, 0:CW * size]))
                if k not in POOL_VALUES:
                    link(nc.vector.tensor_tensor(val, s, a, ALU.subtract))
                    nc.vector.tensor_scalar(half, s, 0.5, None, ALU.mult)
                    link(nc.vector.tensor_tensor(val, a, val, ALU.add))
                else:
                    link(nc.vector.tensor_scalar(half, s, 0.5, None, ALU.mult))
                link(nc.vector.tensor_tensor(a, a, half, ALU.is_gt))
                link(nc.vector.tensor_tensor(val, val, a, ALU.mult))
                nc.vector.tensor_tensor(wq[:, size * n:size * (n + 1), CW * c:CW * (c + 1)], val, sgn, ALU.mult)\
                    .then_inc(wq_ready, 1)

            def quantise_projection(step):
                if step == 0:
                    dve.wait_ge(scale_ready, CHUNKS + 1)
                    link(nc.vector.tensor_scalar(wp_scale[:], wp_scale[:], 1e-8, None, ALU.max))
                    nc.vector.tensor_scalar(wp_half[:], wp_scale[:], 0.5, None, ALU.mult).then_inc(wp_step, 1)
                    return
                dve.wait_ge(wp_step, step)
                s, half = view(wp_scale, 0, (0, R), (1, L)), view(wp_half, 0, (0, R), (1, L))
                if step == 1:
                    ins = nc.vector.tensor_tensor(wpq[:], s, wp_abs[:], ALU.subtract)
                elif step == 2:
                    ins = nc.vector.tensor_tensor(wpq[:], wp_abs[:], wpq[:], ALU.add)
                elif step == 3:
                    ins = nc.vector.tensor_tensor(wp_abs[:], wp_abs[:], half, ALU.is_gt)
                elif step == 4:
                    ins = nc.vector.tensor_tensor(wpq[:], wpq[:], wp_abs[:], ALU.mult)
                else:
                    ins = nc.vector.tensor_tensor(wpq[:], wpq[:], wp_sgn[:], ALU.mult)
                ins.then_inc(wpq_ready if step == WP_STEPS - 1 else wp_step, 1)

            def hidden_scale():
                dve.wait_ge(smax_psum, 1)
                nc.vector.tensor_reduce(s_max[:, 0:1], ps[:, PICK, 0:2 * LB * 2 * HID // P], AX.X, ALU.max)\
                    .then_inc(smax_col, 1)

            def hidden_scale_2():
                dve.wait_ge(smax_all, 1)
                link(nc.vector.reciprocal(s_max[:, 2:3], s_max[:, 1:2]))
                link(nc.vector.scalar_tensor_tensor(h_scale[:, 0:1], s_max[:, 2:3], 0.5, s_max[:, 2:3],
                                                    ALU.mult, ALU.mult))
                link(nc.vector.scalar_tensor_tensor(h_scale[:, 1:2], h_scale[:, 0:1], RMS_EPS, h_scale[:, 0:1],
                                                    ALU.mult, ALU.mult))

            def residual(i, b):
                if i == 0 and b == 0:
                    dve.wait_ge(tanh_ready, 1)
                dve.wait_ge(red_ready, NB * i + b + 1)
                o = (NB * i + b) * L
                nc.vector.scalar_tensor_tensor(
                    view(x1, o, (P, LB), (1, P)), view(ps, (GU + b) * 512 + P - 1, (P, LB), (-1, P)),
                    g_tanh[:, 0:1], view(x_nat, o, (P, LB), (1, P)), ALU.mult, ALU.add).then_inc(x1_ready, 1)

            def second_norm(i):
                for n in range(2):
                    bs = (2 * n, 2 * n + 1)
                    for b in bs:
                        residual(i, b)
                    dve.wait_ge(x1_ready, NB * i + bs[-1] + 1)
                    norm_stats(x1, 2 + i, i, bs)
                for n in range(2):
                    dve.wait_ge(rstd_ready, 3 + 2 * i + n)
                    normalise(x1, 2 + i, i, (2 * n, 2 * n + 1), False)

            def x_low(i):
                for n in range(2):
                    dve.wait_ge(xhi_ready, 2 * i + n + 1)
                    nc.vector.tensor_tensor(turned_x(i, 1, n),
                                            view(ps, (XT + n) * 512, (256, 2), (P, LB), (1, P)),
                                            turned_x(i, 0, n), ALU.subtract).then_inc(xlo_ready, 1)

            def hidden(i, m):
                n = MB * i + m
                dve.wait_ge(up_ready, n + 1)
                dve.wait_ge(silu_ready, n + 1)
                if n >= len(h_val):
                    last = n - len(h_val)
                    dve.wait_ge(hhi_ready, last + 1)
                    dve.wait_ge(hsq_ready, last + 1)
                    dve.wait_ge(hlo_ready[last // MB], last % MB + 1)
                nc.vector.scalar_tensor_tensor(h_val[n % len(h_val)], ps[:, GU + 2 * (n % 2) + 1, :], h_scale[:, 0:1],
                                               silu[:, n % 2, :], ALU.mult, ALU.mult).then_inc(h_ready, 1)

            def mean_squares(i):
                dve.wait_ge(ssq_ready, i + 1)
                nc.vector.tensor_scalar(ms[:, NB * i:NB * (i + 1)], ps[:, OUT[0], L:L + NB], 1.0 / HID, h_scale[:, 1:2],
                                        ALU.mult, ALU.add).then_inc(ms_ready, 1)

            def result(i, b):
                tb = NB * i + b
                dve.wait_ge(coef_ready, i + 1)
                dve.wait_ge(o_ready, tb + 1)
                nc.vector.scalar_tensor_tensor(x1[:, tb, :], ps[:, OUT[b], 0:L], coef[:, tb:tb + 1],
                                               x1[:, tb, :], ALU.mult, ALU.add).then_inc(y_out, 1)

            nc.vector.memset(ones_col[:], 1.0)
            nc.vector.memset(fold_b[:], 0.0)
            rows = 2 * HG * HU * ROWS_B
            nc.vector.memset(view(prod_b, 0, (WIDE, rows), (1, ROWS_B)), 0.0)
            nc.vector.memset(view(prod_b, HD + 1, (WIDE, rows), (1, ROWS_B - 1)), 0.0)
            nc.vector.memset(pick[:], 0.0)
            link(nc.vector.memset(ones64[:], 0.0))
            for n in range(P // GROUP):
                g0 = GROUP * n
                nc.vector.memset(ones64[g0:g0 + GROUP, g0:g0 + GROUP], 1.0)
                nc.vector.memset(pick[g0:g0 + 1, n:n + 1], 1.0).then_inc(sel_ready, 1)
            dve.wait_ge(ident_ready, 1)
            nc.vector.tensor_copy(ident_b[:], ident[:]).then_inc(sel_ready, 1)
            half = tuple(range(NB))
            dve.wait_ge(ld_x[0], 16)
            norm_stats(x_nat, 0, 0, half)
            dve.wait_ge(rstd_ready, 1)
            normalise(x_nat, 0, 0, half, True)
            dve.wait_ge(k_ready[0], 1)
            pair_products(nc.vector, 0, 0)
            pair_products(nc.vector, 0, 1)
            dve.wait_ge(q_ready[0], 1)
            for h in range(H):
                products(0, h)
                if h == 1:
                    pair_products(nc.vector, 0, 2)
                if h == 5:
                    clip(0)
                    clip(1)
                if h == 7:
                    dve.wait_ge(ld_x[1], 16)
                    norm_stats(x_nat, 1, 1, half)
                if h == 13:
                    quantise(0)
                if h == 10:
                    dve.wait_ge(rstd_ready, 2)
                    normalise(x_nat, 1, 1, half, True)
                if h == 13:
                    clip(2)
                    clip(3)
            hidden_scale()
            quantise(1)
            quantise(2)
            second_norm(0)
            dve.wait_ge(q_ready[1], 1)
            x_low(0)
            products(1, 0)
            hidden_scale_2()
            products(1, 1)
            for m in range(MB):
                hidden(0, m)
                if m < MB - 1:
                    products(1, 2 * m + 2)
                    products(1, 2 * m + 3)
                if m < Q_STEPS[3]:
                    quantise(3, m)
                if m == Q_STEPS[3]:
                    quantise_projection(0)
                if m >= Q_STEPS[3] and m != MB - 2:
                    quantise_projection(m - Q_STEPS[3] + 1 if m < MB - 1 else WP_STEPS - 1)
            second_norm(1)
            x_low(1)
            for m in range(MB):
                hidden(1, m)
                if m >= 1:
                    low_part(dve, 1, m - 1)
                if m == 2:
                    mean_squares(0)
                if m > MB - 1 - NB:
                    result(0, m - (MB - NB))
            low_part(dve, 1, MB - 1)
            mean_squares(1)
            for b in range(NB):
                result(1, b)

        @block.tensor
        def _(pe):
            def transpose(dst, src, start=True, stop=True):
                eye = ident if src.dtype == F32 else ident_b
                return nc.tensor.matmul(dst, src, eye[:], start=start, stop=stop, is_transpose=True,
                                        skip_group_check=True)

            def keep_warm(bank, n):
                for _ in range(n):
                    transpose(ps[:, bank, 0:P], ident[:])

            def tp_bank(use):
                if use >= 2:
                    pe.wait_ge(tp_read, use - 1)
                return TP + use % 2

            def heads(src, i, use, normed=False):
                for n in range(2):
                    bank = tp_bank(use + n)
                    if normed:
                        pe.wait_ge(norm_ready, NB * i + 2 * n + 2)
                    for lb in range(LB):
                        for b in range(2):
                            last = transpose(ps[:, bank, 256 * lb + P * b:256 * lb + P * (b + 1)],
                                             src[:, NB * i + 2 * n + b, P * lb:P * (lb + 1)])
                    last.then_inc(tp_written, 1)

            def ctx_heads(i):
                pe.wait_ge(ld_ctx[i], 16)
                heads(c_nat, i, USE_K[i])

            def q_heads(i):
                heads(n_nat, i, USE_Q[i], True)

            def conv(i, h):
                n = H * i + h
                if i == 0 and h % HG == 0:
                    pe.wait_ge(diag_ready, h // HG + 1)
                if h % HG == 0:
                    g = h // HG
                    if i == 0 and g < 3:
                        pe.wait_ge(kv_first, g + 1)
                    else:
                        pe.wait_ge(kv_ready[i], g + 1 if i else 1)
                if n >= 2:
                    pe.wait_ge(y_used, n - 1)
                o, w = h * HU * PAIRS, NB * PAIRS
                bank = YB + n % 2
                nc.tensor.matmul(ps[:, bank, 0:2 * w], toep[:, h, P:2 * P], kv[i][:, o:o + 2 * w], start=True, stop=False)
                nc.tensor.matmul(ps[:, bank, w:2 * w], toep[:, h, 0:P], kv[i][:, o:o + w],
                                 start=False, stop=True).then_inc(y_ready, 1)

            def w_transposes(c):
                half, r0 = c * CW // HID, (c * CW % HID) // P
                if c % 2 == 0:
                    pe.wait_ge(ld_w[half], 16)
                bank = ps[:, tp_bank(USE_W[c]), :].bitcast(BF16)
                for n in range(LB):
                    for r in range(CW // P):
                        o = CW * n + P * r
                        last = transpose(bank[:, o:o + P], w_nat[:, half, r0 + r, P * n:P * (n + 1)])
                last.then_inc(tp_written, 1)

            def group_sums(k):
                c = W_ORDER[k]
                pe.wait_ge(tp_read, USE_W[c] + 1)
                if k >= 2:
                    pe.wait_ge(scale_ready, k - 1)
                bank = GU + 2 * (k % 2)
                for n in range(LB):
                    last = nc.tensor.matmul(ps[:, bank + n, :], ones64[:], w_abs[:, c, CW * n:CW * (n + 1)],
                                            start=True, stop=True)
                last.then_inc(sum_ready, 1)

            def wp_transposes():
                pe.wait_ge(ld_w[2], 16)
                for n in range(2):
                    bank = ps[:, tp_bank(USE_WP + n), :].bitcast(BF16)
                    for r in range(R // 2 * n, R // 2 * (n + 1)):
                        for d in range(LB):
                            o = L * (r % (R // 2)) + P * d
                            last = transpose(bank[:, o:o + P], wp_nat[:, d, r::R])
                    last.then_inc(tp_written, 1)

            def wp_sums():
                pe.wait_ge(consts_ready, 1)
                pe.wait_ge(tp_read, USE_WP + 2)
                pe.wait_ge(scale_ready, CHUNKS)
                for r in range(R):
                    last = nc.tensor.matmul(ps[:, WPS, 0:L], ones8[:], wp_abs[:, r, :], start=(r == 0), stop=(r == R - 1))
                last.then_inc(sum_ready, 1)

            def pick_scales():
                pe.wait_ge(clip_ready, CHUNKS)
                for c in range(CHUNKS):
                    for r in range(LB * CW // P):
                        o = 2 * (LB * CW // P * c + r)
                        last = nc.tensor.matmul(ps[:, PICK, o:o + 2], w_scale[:, c, P * r:P * (r + 1)],
                                                pick[:], start=True, stop=True)
                last.then_inc(smax_psum, 1)

            def reduce_rows(i, second):
                pe.wait_ge(*((sumb_ready, H // HG * (i + 1)) if second else (y_used, H * (i + 1))))
                for b in range(NB):
                    if not second and b in (0, 2):
                        if i == 1:
                            pe.wait_ge(h_ready, MB - 1 + b // 2)
                        elif b == 0:
                            pe.wait_ge(scale_ready, CHUNKS - 1)
                        else:
                            pe.wait_ge(scale_ready, CHUNKS + 1)
                            pe.wait_ge(smax_col, 1)
                    for lb in range(LB):
                        u = lb * NB + b
                        dst = ps[:, GU + b, P * lb:P * (lb + 1)]
                        if second:
                            last = transpose(dst, sum_b[:, u, :], False, lb == LB - 1)
                        else:
                            for r in range(ROWS_A):
                                transpose(dst, prod_a[:, u, r, :], lb == 0 and r == 0, False)
                    if second:
                        last.then_inc(red_ready, 1)

            def x_transposes(i):
                for n in range(2):
                    pe.wait_ge(norm_ready, NB * (2 + i) + 2 * n + 2)
                    for b in range(2):
                        for d in range(LB):
                            last = transpose(ps[:, XT + n, 256 * b + P * d:256 * b + P * (d + 1)],
                                             n_nat[:, NB * i + 2 * n + b, P * d:P * (d + 1)])
                    last.then_inc(xt_psum, 1)

            def gate_up(i, m):
                n = MB * i + m
                bank = GU + 2 * (n % 2)
                if m == 0:
                    pe.wait_ge(xlo_ready, 2 * i + 2)
                if n == 0:
                    pe.wait_ge(wq_ready, sum(Q_STEPS[:2]))
                if n == MB // 2:
                    pe.wait_ge(wq_ready, sum(Q_STEPS))
                if n >= 2:
                    pe.wait_ge(h_ready, n - 1)
                for half, ready in enumerate((gate_ready, up_ready)):
                    for d in range(LB):
                        for part in range(2):
                            last = nc.tensor.matmul(ps[:, bank + half, :],
                                                    wq[:, d, HID * half + P * m:HID * half + P * (m + 1)],
                                                    xt[i][:, part, d, :],
                                                    start=(d == 0 and part == 0), stop=(d == 1 and part == 1))
                    last.then_inc(ready, 1)

            def project(i, b):
                tb = NB * i + b
                bank = OUT[b]
                if i == 1:
                    pe.wait_ge(y_out, b + 1)
                elif b == 0:
                    pe.wait_ge(tp_read, USE_Q[1] + 2)
                    pe.wait_ge(y_used, 2 * H)
                    pe.wait_ge(wpq_ready, 1)
                t = slice(P * b, P * (b + 1))
                for m in range(MB):
                    if b == 0:
                        pe.wait_ge(hhi_ready, MB * i + m + 1)
                    for part in range(2):
                        if b == 0 and part == 1:
                            pe.wait_ge(hlo_ready[i], m + 1)
                        last = nc.tensor.matmul(ps[:, bank, 0:L], (h_hi, h_lo)[part][:, m, t], wpq[:, m, :],
                                                start=(m == 0 and part == 0), stop=(m == MB - 1 and part == 1))
                last.then_inc(o_ready, 1)

            def sum_squares(i):
                pe.wait_ge(hacc_ready, ADDS * (i + 1))
                for b in range(NB):
                    last = nc.tensor.matmul(ps[:, OUT[0], L + b:L + b + 1], h_acc[:, P * b:P * (b + 1)], ones_col[:, 0:1],
                                            start=True, stop=True)
                last.then_inc(ssq_ready, 1)

            pe.wait_ge(ident_ready, 1)
            keep_warm(GU, 18)
            ctx_heads(0)
            q_heads(0)
            keep_warm(GU, 4)
            for h in range(H):
                conv(0, h)
                if h == 1:
                    pe.wait_ge(sel_ready, 3)
                    w_transposes(W_ORDER[0])
                    w_transposes(W_ORDER[1])
                if h == 5:
                    group_sums(0)
                    group_sums(1)
                if h == 7:
                    ctx_heads(1)
                if h == 9:
                    w_transposes(W_ORDER[2])
                    w_transposes(W_ORDER[3])
                if h == 11:
                    group_sums(2)
                if h == 12:
                    group_sums(3)
                if h == 13:
                    wp_transposes()
            pick_scales()
            wp_sums()
            reduce_rows(0, False)
            reduce_rows(0, True)
            q_heads(1)
            conv(1, 0)
            conv(1, 1)
            pe.wait_ge(tp_read, USE_Q[1] + 1)
            keep_warm(TP, 20)
            x_transposes(0)
            keep_warm(TP, 12)
            for m in range(MB):
                gate_up(0, m)
                if m < MB - 1:
                    conv(1, 2 * m + 2)
                    conv(1, 2 * m + 3)
            reduce_rows(1, False)
            reduce_rows(1, True)
            for b in range(NB - 1):
                project(0, b)
            x_transposes(1)
            project(0, NB - 1)
            for m in range(MB):
                gate_up(1, m)
                if m == 1:
                    sum_squares(0)
            project(1, 0)
            project(1, 1)
            sum_squares(1)
            project(1, 2)
            project(1, 3)


def kernel(x, ctx_2048, g_xattn, g_ffn, L0_xattn_ssm_kernel, L0_xattn_D, L0_ffn_w_gate_up, L0_ffn_w_proj):
    import numpy as np
    import concourse.bacc as bacc
    from concourse.bass_utils import run_bass_kernel_spmd

    nc = bacc.Bacc("TRN2", target_bir_lowering=False, num_devices=1)
    turned = np.zeros((H, P + L), np.float32)
    turned[:, :L] = np.asarray(L0_xattn_ssm_kernel)[:, ::-1]
    arrays = {
        "x": x, "ctx_in": ctx_2048, "g_xattn": g_xattn, "g_ffn": g_ffn, "w_turned": turned,
        "d_skip": L0_xattn_D, "w_gu": L0_ffn_w_gate_up, "w_proj": L0_ffn_w_proj,
    }
    arrays = {name: np.ascontiguousarray(a) for name, a in arrays.items()}
    args = [nc.dram_tensor(name, a.shape, mybir.dt.from_np(a.dtype), kind="ExternalInput").ap()
            for name, a in arrays.items()]
    out = nc.dram_tensor("out", (B, D_MODEL, L), F32, kind="ExternalOutput").ap()
    flamingo_layer(nc, *args, out)
    return run_bass_kernel_spmd(nc, [arrays], core_ids=[0]).results[0]["out"]
```
